# Optimizing a Trainium2 kernel written in Bass

```python
import numpy as np
import jax
import jax.numpy as jnp

def _softmax(x, axis=-1):
    return jax.nn.softmax(x, axis=axis)

def _gelu(x):
    return jax.nn.gelu(x, approximate=True)

def _silu(x):
    return jax.nn.silu(x)

def _sigmoid(x):
    return jax.nn.sigmoid(x)

def _layernorm(x, axis=-1, eps=1e-05):
    m = jnp.mean(x, axis=axis, keepdims=True)
    v = jnp.var(x, axis=axis, keepdims=True)
    return (x - m) / jnp.sqrt(v + eps)

def _scatter_add(tgt, idx, src, axis=0):
    return tgt.at[idx].add(src)

def _segment_sum(src, seg, n):
    return jax.ops.segment_sum(src, seg, n)
kernel_name = 'mk_adj_preln_d1_adj_r2_e1ec0a'

def setup_inputs(seed: int=0):
    np.random.seed(seed)
    _w = jnp.asarray

    def _rec_inputs():
        import jax
        import jax.numpy as jnp
        _gk = jax.random.key(seed)
        x = -0.0002928 + 1 * jax.random.normal(jax.random.fold_in(_gk, 1), (2048, 256), jnp.float32)
        _a = jax.random.bernoulli(jax.random.fold_in(_gk, 2), 0.00390625, (2048, 2048))
        _a = jnp.logical_or(_a, jnp.swapaxes(_a, -1, -2))
        _a = jnp.logical_or(_a, jnp.eye(2048, dtype=bool))
        _af = _a.astype(jnp.float32)
        adj = _af
        return (x, adj)
    x, adj = _rec_inputs()

    def _L0_gnn_setup():
        import jax, jax.numpy as jnp
        import numpy as np
        N = 4096
        D = 256
        L = 2
        NEG_SLOPE = 0.01

        def _gat_layer(x, W, adj):
            proj = x @ W
            Wh, Ws = jnp.split(proj, 2, axis=-1)
            scores = Wh @ Ws.T
            a = jax.nn.softmax(scores, axis=-1) * adj
            out = a @ Wh
            out = out + x
            return jax.nn.leaky_relu(out, NEG_SLOPE)
        key = jax.random.key(seed)
        k1, k2, k3 = jax.random.split(key, 3)
        inputs = jax.random.normal(k1, (N, D), dtype=jnp.float32)
        adj = jax.random.randint(k2, (N, N), 0, 2).astype(jnp.float32)
        W_stack = jax.random.normal(k3, (L, D, 2 * D), dtype=jnp.float32) * (1.0 / np.sqrt(D))
        return {'inputs': inputs, 'adj': adj, 'W_stack': W_stack}
    _L0_gnn_all = _L0_gnn_setup()
    _L0_gnn_in = {k: v for k, v in _L0_gnn_all.items() if k in ('W_stack',)}
    del _L0_gnn_all
    return {'x': x, 'adj': adj, 'L0_gnn_W_stack': _L0_gnn_in['W_stack']}

def reference(x, adj, L0_gnn_W_stack):
    import jax
    import jax.numpy as jnp

    def _L0_gnn_ref(inputs, adj, W_stack):
        import jax, jax.numpy as jnp
        import numpy as np
        N = 4096
        D = 256
        L = 2
        NEG_SLOPE = 0.01

        def _gat_layer(x, W, adj):
            proj = x @ W
            Wh, Ws = jnp.split(proj, 2, axis=-1)
            scores = Wh @ Ws.T
            a = jax.nn.softmax(scores, axis=-1) * adj
            out = a @ Wh
            out = out + x
            return jax.nn.leaky_relu(out, NEG_SLOPE)
        x = inputs
        for l in range(W_stack.shape[0]):
            x = _gat_layer(x, W_stack[l], adj)
        return x
    h = jnp.maximum(_layernorm(x, axis=-1), 0.0)
    x = x + _L0_gnn_ref(h, adj, L0_gnn_W_stack)
    return x

_drawn_inputs = setup_inputs


def setup_inputs(seed=0):
    import zlib

    import numpy as np

    out = dict(_drawn_inputs(seed))
    spreads = {}
    factors = {}
    for name, (base, spread) in spreads.items():
        noise = np.random.default_rng([zlib.crc32(name.encode()), seed]).standard_normal(out[name].shape)
        drawn = base * np.exp(spread * noise) if base else spread * noise
        out[name] = jnp.asarray(drawn.astype(out[name].dtype))
    for name, factor in factors.items():
        out[name] = (out[name] * factor).astype(out[name].dtype)
    return out
```

```python
import concourse.bass as bass
from concourse import mybir
from contextlib import ExitStack

P = 128
N, D, LAYERS = 2048, 256, 2
TILES = N // P
KD = D // P
BANK = 512
CHUNKS = N // BANK
TPC = BANK // P
HI, LO = 0, 1
PASSES = ((HI, HI), (HI, LO), (LO, HI))
EPS = 1e-05
SLOPE = 0.01

F32 = mybir.dt.float32
F32R = mybir.dt.float32r
ALU = mybir.AluOpType
ACT = mybir.ActivationFunctionType
AX = mybir.AxisListType


def gat_kernel(nc, x, adj, weights, out):
    ctx = ExitStack()
    with ctx:
        def sb(name, shape, dt=F32):
            return ctx.enter_context(nc.sbuf_tensor(name, shape, dt))

        def sem(name):
            return ctx.enter_context(nc.semaphore(name))

        hT = sb("hT", [P, 2, KD, N], F32R)
        wsT = sb("wsT", [P, 2, KD, N], F32R)
        wh_nat = sb("wh_nat", [P, TILES, 2, D], F32R)
        h_nat = sb("h_nat", [P, TILES, D])
        adj_sb = sb("adj_sb", [P, 2, N])
        probs = sb("probs", [P, 2, N])
        pT = sb("pT", [P, 2, TILES, P], F32R)
        wh_tile = sb("wh_tile", [P, 2, 2, KD, P], F32R)
        w_raw = sb("w_raw", [P, KD, 2 * D])
        w_hl = sb("w_hl", [P, 2, KD, 2 * D], F32R)
        h_new = sb("h_new", [P, 2, D])
        z = sb("z", [P, D])
        x_tile = sb("x_tile", [P, 2, D])
        ident = sb("ident", [P, P])
        ident_r = sb("ident_r", [P, P], F32R)
        negmax = sb("negmax", [P, 1])
        rowsum = sb("rowsum", [P, 2, 1])
        rinv = sb("rinv", [P, 1])
        stats = sb("stats", [P, TPC, 6])
        meanvar = sb("meanvar", [P, TPC, 2])
        var_eps = sb("var_eps", [P, TPC, 1])
        std0 = sb("std0", [P, TPC, 1])
        std_inv0 = sb("std_inv0", [P, TPC, 1])
        quot = sb("quot", [P, TPC, 1])
        std = sb("std", [P, TPC, 1])
        rstd = sb("rstd", [P, TPC, 1])

        ps = ctx.enter_context(nc.psum_tensor("ps", [P, 8, BANK], F32))
        scores = ps[:, 0:CHUNKS, :].rearrange("p c n -> p (c n)")

        def tbank(q):
            return ps[:, CHUNKS + q % 2, :]

        def prod(par):
            return ps[:, CHUNKS + 2 + par, 0:D]

        def hTbank(par):
            return ps[:, CHUNKS + 2 + par, D:2 * D]

        def bits(ap):
            return ap.bitcast(F32)

        x_in = [sem(f"x_in{c}") for c in range(CHUNKS)]
        w_in = [sem(f"w_in{n}") for n in range(LAYERS)]
        adj_in = [sem(f"adj_in{b}") for b in range(2)]
        xt_in = [sem(f"xt_in{b}") for b in range(2)]
        stored = [sem(f"stored{b}") for b in range(2)]
        ident_done = sem("ident_done")
        identr_done = sem("identr_done")
        stats_done = sem("stats_done")
        aggr_done = sem("aggr_done")
        vareps_done = sem("vareps_done")
        sqrt_done = sem("sqrt_done")
        newton_done = sem("newton_done")
        centred_done = sem("centred_done")
        ln_ready = sem("ln_ready")
        w_hi = sem("w_hi")
        w_lo = sem("w_lo")
        hT_done = sem("hT_done")
        hT_hi = sem("hT_hi")
        hT_lo = sem("hT_lo")
        saved = sem("saved")
        proj_done = sem("proj_done")
        proj_hi = sem("proj_hi")
        proj_lo = sem("proj_lo")
        nat_done = sem("nat_done")
        nat_act = sem("nat_act")
        nat_dve = sem("nat_dve")
        tile_ready = sem("tile_ready")
        scores_done = sem("scores_done")
        max_done = sem("max_done")
        exp_done = sem("exp_done")
        mask_done = sem("mask_done")
        tr_done = sem("tr_done")
        pT_hi = sem("pT_hi")
        pT_lo = sem("pT_lo")
        prod_done = sem("prod_done")
        rinv_done = sem("rinv_done")
        z_done = sem("z_done")
        leaky_done = sem("leaky_done")
        h_ready = sem("h_ready")

        block = ctx.enter_context(nc.Block())

        def two(eng, first, last, step):
            with eng.Fori(first, last, 2) as i:
                step(i, 0)
                step(i + 1, 1)

        @block.sync
        def _(sp):
            for c in range(CHUNKS):
                sp.dma_start(h_nat[:, TPC * c:TPC * (c + 1), :],
                             x[BANK * c:BANK * (c + 1), :].rearrange("(t p) d -> p t d", p=P)).then_inc(x_in[c], 16)
            sp.dma_start(w_raw[:, :, :], weights[0].rearrange("(k p) n -> p k n", p=P)).then_inc(w_in[0], 16)

            def load_adj(i, par):
                sp.dma_start(adj_sb[:, par, :], adj[bass.ds(i * P, P), :]).then_inc(adj_in[par], 16)

            load_adj(0, 0)
            load_adj(1, 1)
            sp.wait_ge(w_lo, 1)
            sp.dma_start(w_raw[:, :, :], weights[1].rearrange("(k p) n -> p k n", p=P)).then_inc(w_in[1], 16)

            def next_adj(layer, i, par):
                sp.wait_ge(mask_done, layer * TILES + i - 1)
                load_adj(i, par)

            two(sp, 2, TILES - 1, lambda i, par: next_adj(0, i, par))

            def load_x(i, par):
                sp.dma_start(x_tile[:, par, :], x[bass.ds(i * P, P), :]).then_inc(xt_in[par], 16)

            def store(i, par):
                sp.wait_ge(h_ready, TILES + i + 1)
                sp.dma_start(out[bass.ds(i * P, P), :], h_new[:, par, :]).then_inc(stored[par], 16)

            load_x(0, 0)
            load_x(1, 1)
            next_adj(1, 0, 0)
            next_adj(1, 1, 1)
            next_adj(1, 2, 0)
            next_adj(1, 3, 1)
            store(0, 0)
            load_x(2, 0)

            def step(i, par):
                next_adj(1, i, par)
                store(i - 3, 1 - par)
                load_x(i - 1, 1 - par)

            two(sp, 4, TILES - 1, step)
            store(TILES - 3, 1)
            load_x(TILES - 1, 1)
            store(TILES - 2, 0)
            store(TILES - 1, 1)
            for b in range(2):
                sp.wait_ge(stored[b], 16 * (TILES // 2))

        @block.gpsimd
        def _(pool):
            nc.gpsimd.memset(ident[:, :], 0.0).then_inc(ident_done, 1)
            pool.wait_ge(ident_done, 1)
            nc.gpsimd.affine_select(out=ident[:, :], in_=ident[:, :], compare_op=ALU.not_equal, fill=1.0,
                                    base=0, pattern=[[-1, P]], channel_multiplier=1).then_inc(ident_done, 1)

            def save_h(n, i, par, ready, count):
                pool.wait_ge(ready, count)
                nc.gpsimd.tensor_copy(h_nat[:, bass.ds(i, 1), :].rearrange("p a d -> p (a d)"),
                                      h_new[:, par, :]).then_inc(saved, 1)

            for i in range(TILES):
                save_h(i, i, i % 2, ln_ready, i + 1)

            def take_tile(layer, i, par):
                if not (layer == 0 and isinstance(i, int) and i < 2):
                    pool.wait_ge(scores_done, layer * TILES + i - 1)
                nc.gpsimd.tensor_copy(
                    wh_tile[:, par, :, :, :].rearrange("p h k n -> p (h k) n"),
                    hT[:, :, :, bass.ds(i * P, P)].rearrange("p h k n -> p (h k) n")).then_inc(tile_ready, 1)

            for layer in range(LAYERS):
                pool.wait_ge(proj_lo, 4 * CHUNKS * (layer + 1))
                take_tile(layer, 0, 0)
                take_tile(layer, 1, 1)
                if layer == 0:
                    def step(i, par):
                        take_tile(0, i, par)
                        save_h(TILES + i - 2, i - 2, par, h_ready, i - 1)

                    two(pool, 2, TILES - 1, step)
                    save_h(2 * TILES - 2, TILES - 2, 0, h_ready, TILES - 1)
                    save_h(2 * TILES - 1, TILES - 1, 1, h_ready, TILES)
                else:
                    two(pool, 2, TILES - 1, lambda i, par: take_tile(1, i, par))

        @block.tensor
        def _(pe):
            def transpose_h(n, par, ready, count, first=False):
                pe.wait_ge(ready, count)
                if not first:
                    pe.wait_ge(hT_lo, n - 1)
                for k in range(KD):
                    last = nc.tensor.transpose(hTbank(par)[:, k * P:(k + 1) * P],
                                               h_new[:, par, k * P:(k + 1) * P], ident[:, :])
                last.then_inc(hT_done, 1)

            def proj_bank(layer, c, b):
                if b == 0:
                    pe.wait_ge(hT_lo, TILES * layer + TPC * (c + 1))
                    if c == 0:
                        pe.wait_ge(w_lo, layer + 1)
                        if layer:
                            pe.wait_ge(exp_done, TILES * layer)
                if c > 0:
                    pe.wait_ge(proj_lo, 4 * (CHUNKS * layer + c - 1) + b + 1)
                m = (b + KD) % (2 * KD)
                n = 0
                for k in range(KD):
                    for wh, mh in PASSES:
                        last = nc.tensor.matmul(ps[:, b, :], w_hl[:, wh, k, m * P:(m + 1) * P],
                                                hT[:, mh, k, c * BANK:(c + 1) * BANK],
                                                start=(n == 0), stop=(n == KD * len(PASSES) - 1))
                        n += 1
                last.then_inc(proj_done, 1)

            def nat(layer, i):
                pe.wait_ge(proj_lo, 4 * (CHUNKS * layer + i // TPC + 1))
                if i >= 2:
                    pe.wait_ge((nat_act, nat_dve)[i % 2], (TILES * layer + i) // 2)
                elif layer:
                    pe.wait_ge(pT_lo, 4 * TILES * layer)
                dst = tbank(i).bitcast(F32R)
                for n, (half, k) in enumerate(((HI, 0), (HI, 1), (LO, 0), (LO, 1))):
                    last = nc.tensor.transpose(dst[:, n * P:(n + 1) * P], hT[:, half, k, i * P:(i + 1) * P],
                                               ident_r[:, :])
                last.then_inc(nat_done, 1)

            def project(layer, c, after_two=None):
                for b in (0, 1):
                    proj_bank(layer, c, b)
                if c:
                    nat(layer, TPC * (c - 1))
                    nat(layer, TPC * (c - 1) + 1)
                if after_two:
                    after_two()
                for b in (2, 3):
                    proj_bank(layer, c, b)
                    if c:
                        nat(layer, TPC * (c - 1) + b)

            def score_chunk(layer, i, par, q):
                if q == 0:
                    pe.wait_ge(tile_ready, TILES * layer + i + 1)
                    if not (isinstance(i, int) and i == 0):
                        pe.wait_ge(exp_done, TILES * layer + i)
                if isinstance(i, int) and i == 0:
                    pe.wait_ge(proj_lo, 4 * (CHUNKS * (layer + 1) - 1) + max(q + 1, 2 if q == CHUNKS - 1 else 0))
                n = 0
                for k in range(KD):
                    for sh, mh in PASSES:
                        last = nc.tensor.matmul(ps[:, q, :], wh_tile[:, par, sh, k, :],
                                                wsT[:, mh, k, q * BANK:(q + 1) * BANK],
                                                start=(n == 0), stop=(n == KD * len(PASSES) - 1))
                        n += 1
                if q == CHUNKS - 1:
                    last.then_inc(scores_done, 1)

            def transpose_group(layer, i, par, q):
                g = TILES * layer + i
                if q == 0:
                    pe.wait_ge(mask_done, g + 1)
                if isinstance(i, int) and i == 0 and q < 2:
                    pe.wait_ge((nat_act, nat_dve)[q], (layer + 1) * TILES // 2)
                else:
                    pe.wait_ge(pT_lo, 4 * g + q - 1)
                for t in range(TPC):
                    j = q * TPC + t
                    last = nc.tensor.transpose(tbank(q)[:, t * P:(t + 1) * P],
                                               probs[:, par, j * P:(j + 1) * P], ident[:, :])
                last.then_inc(tr_done, 1)

            def product_quarter(layer, i, par, q):
                g = TILES * layer + i
                pe.wait_ge(pT_lo, 4 * g + q + 1)
                if q == 0:
                    if isinstance(i, int) and i == 0:
                        pe.wait_ge(nat_act, (layer + 1) * TILES // 2)
                        pe.wait_ge(nat_dve, (layer + 1) * TILES // 2)
                    if not (isinstance(i, int) and i < 2):
                        pe.wait_ge(h_ready, g - 1)
                        if layer == 0:
                            pe.wait_ge(hT_lo, TILES + i - 1)
                    elif layer == 0:
                        pe.wait_ge(hT_lo, TILES)
                    else:
                        pe.wait_ge(hT_lo, 2 * TILES)
                for t in range(TPC):
                    j = q * TPC + t
                    for n, (sh, mh) in enumerate(PASSES):
                        last = nc.tensor.matmul(prod(par), pT[:, sh, j, :], wh_nat[:, j, mh, :],
                                                start=(j == 0 and n == 0),
                                                stop=(j == TILES - 1 and n == len(PASSES) - 1))
                if q == CHUNKS - 1:
                    last.then_inc(prod_done, 1)

            def cycle(layer, i, par, head, with_hT=True):
                head(0)
                head(1)
                transpose_group(layer, i - 1, 1 - par, 0)
                head(2)
                if with_hT:
                    transpose_h(TILES + i - 2, par, h_ready, i - 1)
                transpose_group(layer, i - 1, 1 - par, 1)
                head(3)
                transpose_group(layer, i - 1, 1 - par, 2)
                product_quarter(layer, i - 1, 1 - par, 0)
                transpose_group(layer, i - 1, 1 - par, 3)
                for q in range(1, CHUNKS):
                    product_quarter(layer, i - 1, 1 - par, q)

            pe.wait_ge(ident_done, 2)
            pe.wait_ge(identr_done, 1)
            for c in range(CHUNKS):
                for t in range(TPC):
                    i = TPC * c + t
                    transpose_h(i, i % 2, ln_ready, i + 1, first=i < 2)
                project(0, c)
            for layer in range(LAYERS):
                score_chunk(layer, 0, 0, 0)
                score_chunk(layer, 0, 0, 1)
                nat(layer, TILES - 4)
                nat(layer, TILES - 3)
                score_chunk(layer, 0, 0, 2)
                nat(layer, TILES - 2)
                score_chunk(layer, 0, 0, 3)
                nat(layer, TILES - 1)
                cycle(layer, 1, 1, lambda q: score_chunk(layer, 1, 1, q), with_hT=False)
                two(pe, 2, TILES - 1,
                    lambda i, par: cycle(layer, i, par, lambda q: score_chunk(layer, i, par, q), with_hT=layer == 0))
                if layer + 1 < LAYERS:
                    cycle(layer, TILES, 0, lambda q: proj_bank(layer + 1, 0, q))
                    project(layer + 1, 1,
                            after_two=lambda: transpose_h(2 * TILES - 1, 1, h_ready, TILES))
                    for c in range(2, CHUNKS):
                        project(layer + 1, c)
                else:
                    cycle(layer, TILES, 0, lambda q: None, with_hT=False)

        @block.scalar
        def _(act):
            def copy(dst, src):
                return nc.scalar.activation(dst, src, ACT.Copy)

            def split_w(layer):
                act.wait_ge(w_in[layer], 16)
                if layer:
                    act.wait_ge(proj_done, 4 * CHUNKS)
                copy(w_hl[:, HI, :, :], w_raw[:, :, :]).then_inc(w_hi, 1)

            def hi_hT(n, i, par):
                act.wait_ge(hT_done, n + 1)
                copy(hT[:, HI, :, bass.ds(i * P, P)],
                     hTbank(par).rearrange("p (k n) -> p k n", k=KD)).then_inc(hT_hi, 1)

            def hi_proj(layer, c, b):
                act.wait_ge(proj_done, 4 * (CHUNKS * layer + c) + (b + 1 if b < 2 else 4))
                dst = wsT if b < KD else hT
                copy(dst[:, HI, b % KD, c * BANK:(c + 1) * BANK], ps[:, b, :]).then_inc(proj_hi, 1)

            def nat(layer, i):
                act.wait_ge(nat_done, TILES * layer + i + 1)
                copy(wh_nat[:, i, :, :].rearrange("p h d -> p (h d)"), tbank(i)).then_inc(nat_act, 1)

            def project(layer, c, after_two=None):
                hi_proj(layer, c, 0)
                hi_proj(layer, c, 1)
                if c:
                    nat(layer, TPC * (c - 1))
                if after_two:
                    after_two()
                if c:
                    nat(layer, TPC * (c - 1) + 2)
                hi_proj(layer, c, 2)
                hi_proj(layer, c, 3)

            def exps(layer, i, par):
                act.wait_ge(max_done, TILES * layer + i + 1)
                nc.scalar.activation(probs[:, par, :], scores, ACT.Exp, bias=negmax[:, :],
                                     accum_out=rowsum[:, par, :]).then_inc(exp_done, 1)

            def hi_pT(layer, i, q):
                g = TILES * layer + i
                act.wait_ge(tr_done, 4 * g + q + 1)
                if q == 0 and not (layer == 0 and isinstance(i, int) and i == 0):
                    act.wait_ge(prod_done, g)
                copy(pT[:, HI, q * TPC:(q + 1) * TPC, :].rearrange("p j n -> p (j n)"), tbank(q)).then_inc(pT_hi, 1)

            def cycle(layer, i, par, with_hT=True, with_scores=True):
                hi_pT(layer, i - 1, 0)
                if with_hT:
                    hi_hT(TILES + i - 2, i - 2, par)
                hi_pT(layer, i - 1, 1)
                hi_pT(layer, i - 1, 2)
                hi_pT(layer, i - 1, 3)
                if with_scores:
                    exps(layer, i, par)

            split_w(0)
            for c in range(CHUNKS):
                act.wait_ge(vareps_done, c + 1)
                nc.scalar.activation(std0[:, :, :], var_eps[:, :, :], ACT.Sqrt).then_inc(sqrt_done, 1)
                for t in range(TPC):
                    i = TPC * c + t
                    act.wait_ge(centred_done, i + 1)
                    if i >= 2:
                        act.wait_ge(hT_done, i - 1)
                        act.wait_ge(saved, i - 1)
                    nc.scalar.activation(h_new[:, i % 2, :], h_nat[:, i, :], ACT.Relu, scale=2.0).then_inc(ln_ready, 1)
                    hi_hT(i, i, i % 2)
                project(0, c)
            for layer in range(LAYERS):
                nat(layer, TILES - 4)
                nat(layer, TILES - 2)
                exps(layer, 0, 0)
                cycle(layer, 1, 1, with_hT=False)
                two(act, 2, TILES - 1, lambda i, par: cycle(layer, i, par, with_hT=layer == 0))
                if layer + 1 < LAYERS:
                    split_w(layer + 1)
                    hi_proj(layer + 1, 0, 0)
                    hi_proj(layer + 1, 0, 1)
                    hi_pT(layer, TILES - 1, 0)
                    hi_hT(2 * TILES - 2, TILES - 2, 0)
                    hi_pT(layer, TILES - 1, 1)
                    hi_proj(layer + 1, 0, 2)
                    hi_proj(layer + 1, 0, 3)
                    hi_pT(layer, TILES - 1, 2)
                    hi_pT(layer, TILES - 1, 3)
                    project(layer + 1, 1, after_two=lambda: hi_hT(2 * TILES - 1, TILES - 1, 1))
                    for c in range(2, CHUNKS):
                        project(layer + 1, c)
                else:
                    cycle(layer, TILES, 0, with_hT=False, with_scores=False)

        @block.vector
        def _(dve):
            def rest(dst, src, hi):
                return nc.vector.tensor_tensor(dst, src, bits(hi), ALU.subtract)

            def split_w(layer):
                dve.wait_ge(w_hi, layer + 1)
                rest(w_hl[:, LO, :, :].rearrange("p k n -> p (k n)"), w_raw[:, :, :].rearrange("p k n -> p (k n)"),
                     w_hl[:, HI, :, :].rearrange("p k n -> p (k n)")).then_inc(w_lo, 1)

            def lo_hT(n, i, par):
                dve.wait_ge(hT_hi, n + 1)
                rest(hT[:, LO, :, bass.ds(i * P, P)], hTbank(par).rearrange("p (k n) -> p k n", k=KD),
                     hT[:, HI, :, bass.ds(i * P, P)]).then_inc(hT_lo, 1)

            def lo_proj(layer, c, b):
                dve.wait_ge(proj_hi, 4 * (CHUNKS * layer + c) + b + 1)
                dst = wsT if b < KD else hT
                cols = slice(c * BANK, (c + 1) * BANK)
                rest(dst[:, LO, b % KD, cols], ps[:, b, :], dst[:, HI, b % KD, cols]).then_inc(proj_lo, 1)

            def nat(layer, i):
                dve.wait_ge(nat_done, TILES * layer + i + 1)
                nc.vector.tensor_copy(wh_nat[:, i, :, :].rearrange("p h d -> p (h d)"), tbank(i)).then_inc(nat_dve, 1)

            def project(layer, c, after_two=None):
                lo_proj(layer, c, 0)
                lo_proj(layer, c, 1)
                if c:
                    nat(layer, TPC * (c - 1) + 1)
                if after_two:
                    after_two()
                lo_proj(layer, c, 2)
                lo_proj(layer, c, 3)
                if c:
                    nat(layer, TPC * (c - 1) + 3)

            def maxima(layer, i):
                dve.wait_ge(scores_done, TILES * layer + i + 1)
                nc.vector.tensor_reduce(negmax[:, :], scores, AX.X, ALU.max, negate=True).then_inc(max_done, 1)

            def mask(layer, i, par):
                g = TILES * layer + i
                dve.wait_ge(exp_done, g + 1)
                dve.wait_ge(adj_in[par], 8 * (g - par) + 16)
                nc.vector.tensor_tensor(probs[:, par, :], probs[:, par, :], adj_sb[:, par, :],
                                        ALU.mult).then_inc(mask_done, 1)

            def lo_pT(layer, i, q):
                dve.wait_ge(pT_hi, 4 * (TILES * layer + i) + q + 1)
                js = slice(q * TPC, (q + 1) * TPC)
                rest(pT[:, LO, js, :].rearrange("p j n -> p (j n)"), tbank(q),
                     pT[:, HI, js, :].rearrange("p j n -> p (j n)")).then_inc(pT_lo, 1)

            def tail(layer, i, par):
                g = TILES * layer + i
                nc.vector.reciprocal(rinv[:, :], rowsum[:, par, :]).then_inc(rinv_done, 1)
                dve.wait_ge(rinv_done, g + 1)
                dve.wait_ge(prod_done, g + 1)
                nc.vector.scalar_tensor_tensor(
                    out=z[:, :], in0=prod(par), scalar=rinv[:, :],
                    in1=h_nat[:, bass.ds(i, 1), :].rearrange("p a d -> p (a d)"),
                    op0=ALU.mult, op1=ALU.add).then_inc(z_done, 1)
                dve.wait_ge(z_done, g + 1)
                early = isinstance(i, int) and i < 2
                if layer == 0:
                    dve.wait_ge(hT_done, TILES + i - 1)
                    dve.wait_ge(saved, TILES + i - 1)
                elif early:
                    dve.wait_ge(hT_done, 2 * TILES)
                    dve.wait_ge(saved, 2 * TILES)
                else:
                    dve.wait_ge(stored[par], 8 * (i - par))
                ins = nc.vector.scalar_tensor_tensor(out=h_new[:, par, :], in0=z[:, :], scalar=SLOPE, in1=z[:, :],
                                                     op0=ALU.mult, op1=ALU.max)
                if layer + 1 < LAYERS:
                    ins.then_inc(h_ready, 1)
                else:
                    ins.then_inc(leaky_done, 1)
                    dve.wait_ge(leaky_done, i + 1)
                    dve.wait_ge(xt_in[par], 8 * (i - par) + 16)
                    nc.vector.tensor_tensor(h_new[:, par, :], h_new[:, par, :], x_tile[:, par, :],
                                            ALU.add).then_inc(h_ready, 1)

            def cycle(layer, i, par, with_tail=True, with_scores=True):
                if with_tail:
                    tail(layer, i - 2, par)
                lo_pT(layer, i - 1, 0)
                if with_tail and layer == 0:
                    lo_hT(TILES + i - 2, i - 2, par)
                lo_pT(layer, i - 1, 1)
                if with_scores:
                    maxima(layer, i)
                lo_pT(layer, i - 1, 2)
                lo_pT(layer, i - 1, 3)
                if with_scores:
                    mask(layer, i, par)

            dve.wait_ge(ident_done, 2)
            nc.vector.tensor_copy(ident_r[:, :], ident[:, :]).then_inc(identr_done, 1)
            for c in range(CHUNKS):
                dve.wait_ge(x_in[c], 16)
                for t in range(TPC):
                    nc.vector.bn_stats(stats[:, t, :], h_nat[:, TPC * c + t, :]).then_inc(stats_done, 1)
                for t in range(TPC):
                    dve.wait_ge(stats_done, TPC * c + t + 1)
                    nc.vector.bn_aggr(meanvar[:, t, :], stats[:, t, :]).then_inc(aggr_done, 1)
                dve.wait_ge(aggr_done, TPC * (c + 1))
                nc.vector.tensor_scalar_add(var_eps[:, :, :], meanvar[:, :, 1:2], EPS).then_inc(vareps_done, 1)
                dve.wait_ge(sqrt_done, c + 1)
                nc.vector.reciprocal(std_inv0[:, :, :], std0[:, :, :]).then_inc(newton_done, 1)
                dve.wait_ge(newton_done, 4 * c + 1)
                nc.vector.tensor_tensor(quot[:, :, :], var_eps[:, :, :], std_inv0[:, :, :],
                                        ALU.mult).then_inc(newton_done, 1)
                dve.wait_ge(newton_done, 4 * c + 2)
                nc.vector.scalar_tensor_tensor(
                    out=std[:, :, :].rearrange("p t a -> p (t a)"), in0=std0[:, :, :].rearrange("p t a -> p (t a)"),
                    scalar=1.0, in1=quot[:, :, :].rearrange("p t a -> p (t a)"),
                    op0=ALU.mult, op1=ALU.add).then_inc(newton_done, 1)
                dve.wait_ge(newton_done, 4 * c + 3)
                nc.vector.reciprocal(rstd[:, :, :], std[:, :, :]).then_inc(newton_done, 1)
                dve.wait_ge(newton_done, 4 * c + 4)
                for t in range(TPC):
                    i = TPC * c + t
                    nc.vector.tensor_scalar(h_nat[:, i, :], h_nat[:, i, :], meanvar[:, t, 0:1], rstd[:, t, :],
                                            ALU.subtract, ALU.mult).then_inc(centred_done, 1)
                if c == 0:
                    split_w(0)
                for t in range(TPC):
                    i = TPC * c + t
                    lo_hT(i, i, i % 2)
                project(0, c)
            for layer in range(LAYERS):
                nat(layer, TILES - 3)
                nat(layer, TILES - 1)
                maxima(layer, 0)
                mask(layer, 0, 0)
                cycle(layer, 1, 1, with_tail=False)
                two(dve, 2, TILES - 1, lambda i, par: cycle(layer, i, par))
                if layer + 1 < LAYERS:
                    split_w(layer + 1)
                    tail(layer, TILES - 2, 0)
                    lo_proj(layer + 1, 0, 0)
                    lo_proj(layer + 1, 0, 1)
                    lo_pT(layer, TILES - 1, 0)
                    lo_hT(2 * TILES - 2, TILES - 2, 0)
                    lo_pT(layer, TILES - 1, 1)
                    lo_proj(layer + 1, 0, 2)
                    lo_proj(layer + 1, 0, 3)
                    lo_pT(layer, TILES - 1, 2)
                    lo_pT(layer, TILES - 1, 3)
                    tail(layer, TILES - 1, 1)
                    project(layer + 1, 1, after_two=lambda: lo_hT(2 * TILES - 1, TILES - 1, 1))
                    for c in range(2, CHUNKS):
                        project(layer + 1, c)
                else:
                    cycle(layer, TILES, 0, with_scores=False)
                    tail(layer, TILES - 1, 1)


def kernel(x, adj, L0_gnn_W_stack):
    import numpy as np
    import concourse.bacc as bacc
    from concourse.bass_utils import run_bass_kernel_spmd

    nc = bacc.Bacc("TRN2", target_bir_lowering=False, num_devices=1)
    arrays = {"x": np.ascontiguousarray(x), "adj": np.ascontiguousarray(adj),
              "weights": np.ascontiguousarray(L0_gnn_W_stack)}
    aps = [nc.dram_tensor(n, a.shape, mybir.dt.from_np(a.dtype), kind="ExternalInput").ap()
           for n, a in arrays.items()]
    out = nc.dram_tensor("out", (N, D), F32, kind="ExternalOutput").ap()
    gat_kernel(nc, *aps, out)
    result = run_bass_kernel_spmd(nc, [arrays], core_ids=[0])
    return result.results[0]["out"]
```

```python
import concourse.bass as bass
from concourse import mybir
from contextlib import ExitStack

P = 128
N, D, LAYERS = 2048, 256, 2
TILES = N // P
KD = D // P
BANK = 512
CHUNKS = N // BANK
TPC = BANK // P
HI, LO = 0, 1
PASSES = ((HI, HI), (HI, LO), (LO, HI))
X_LOADS = ((0, 2), (2, 4), (4, 8), (8, 12), (12, 16))
EPS = 1e-05
SLOPE = 0.01

F32 = mybir.dt.float32
F32R = mybir.dt.float32r
ALU = mybir.AluOpType
ACT = mybir.ActivationFunctionType
AX = mybir.AxisListType


def gat_kernel(nc, x, adj, weights, out):
    ctx = ExitStack()
    with ctx:
        def sb(name, shape, dt=F32):
            return ctx.enter_context(nc.sbuf_tensor(name, shape, dt))

        def sem(name):
            return ctx.enter_context(nc.semaphore(name))

        hT = sb("hT", [P, 2, KD, N], F32R)
        wsT = sb("wsT", [P, 2, KD, N], F32R)
        wh_nat = sb("wh_nat", [P, TILES, 2, D], F32R)
        h_nat = sb("h_nat", [P, TILES, D])
        adj_sb = sb("adj_sb", [P, 2, N])
        probs = sb("probs", [P, 2, N])
        pT = sb("pT", [P, 2, TILES, P], F32R)
        wh_tile = sb("wh_tile", [P, 2, 2, KD, P], F32R)
        w_raw = sb("w_raw", [P, KD, 2 * D])
        w_hl = sb("w_hl", [P, 2, KD, 2 * D], F32R)
        h_new = sb("h_new", [P, 2, D])
        z = sb("z", [P, D])
        x_tile = sb("x_tile", [P, 2, D])
        ident = sb("ident", [P, P])
        ident_r = sb("ident_r", [P, P], F32R)
        warm = sb("warm", [P, 1])
        negmax = sb("negmax", [P, 1])
        chunkmax = sb("chunkmax", [P, CHUNKS])
        chunksum = sb("chunksum", [P, 2, CHUNKS])
        rowsum = sb("rowsum", [P, 1])
        rinv = sb("rinv", [P, 2, 1])
        stats = sb("stats", [P, CHUNKS, TPC, 6])
        meanvar = sb("meanvar", [P, CHUNKS, TPC, 2])
        var_eps = sb("var_eps", [P, CHUNKS, TPC])
        std0 = sb("std0", [P, CHUNKS, TPC])
        std_inv0 = sb("std_inv0", [P, CHUNKS, TPC])
        quot = sb("quot", [P, CHUNKS, TPC])
        std = sb("std", [P, CHUNKS, TPC])
        rstd = sb("rstd", [P, CHUNKS, TPC])
        shift = sb("shift", [P, CHUNKS, TPC])

        ps = ctx.enter_context(nc.psum_tensor("ps", [P, 8, BANK], F32))
        def tbank(q):
            return ps[:, CHUNKS + q % 2, :]

        def prod(par):
            return ps[:, CHUNKS + 2 + par, 0:D]

        def hTbank(par):
            return ps[:, CHUNKS + 2 + par, D:2 * D]

        def pair_bank(u):
            return ps[:, CHUNKS + 2 + u % 2, :].rearrange("p (k n) -> p k n", k=KD)

        def score_bank(i, q):
            return CHUNKS + 3 if isinstance(i, int) and i == 1 and q == 0 else q

        def bits(ap):
            return ap.bitcast(F32)

        x_in = [sem(f"x_in{n}") for n in range(len(X_LOADS))]
        w_in = [sem(f"w_in{n}") for n in range(LAYERS)]
        adj_in = [sem(f"adj_in{b}") for b in range(2)]
        xt_in = [sem(f"xt_in{b}") for b in range(2)]
        stored = [sem(f"stored{b}") for b in range(2)]
        ident_done = sem("ident_done")
        identr_done = sem("identr_done")
        stats_done = sem("stats_done")
        aggr_done = sem("aggr_done")
        vareps_done = sem("vareps_done")
        sqrt_done = sem("sqrt_done")
        newton_done = sem("newton_done")
        shift_done = sem("shift_done")
        ln_ready = sem("ln_ready")
        pair_done = sem("pair_done")
        pair_hi = sem("pair_hi")
        pair_lo = sem("pair_lo")
        w_hi = sem("w_hi")
        w_lo = sem("w_lo")
        hT_done = sem("hT_done")
        hT_hi = sem("hT_hi")
        hT_lo = sem("hT_lo")
        saved = sem("saved")
        proj_done = sem("proj_done")
        proj_hi = sem("proj_hi")
        proj_lo = sem("proj_lo")
        nat_done = sem("nat_done")
        nat_out = sem("nat_out")
        tile_ready = sem("tile_ready")
        scores_done = sem("scores_done")
        chunkmax_done = sem("chunkmax_done")
        max_done = sem("max_done")
        exp_done = sem("exp_done")
        mask_done = sem("mask_done")
        tr_done = sem("tr_done")
        pT_hi = sem("pT_hi")
        pT_lo = sem("pT_lo")
        prod_done = sem("prod_done")
        rowsum_done = sem("rowsum_done")
        rinv_done = sem("rinv_done")
        z_done = sem("z_done")
        leaky_done = sem("leaky_done")
        h_ready = sem("h_ready")

        block = ctx.enter_context(nc.Block())

        def two(eng, first, last, step):
            with eng.Fori(first, last, 2) as i:
                step(i, 0)
                step(i + 1, 1)

        @block.sync
        def _(sp):
            for n, (first, end) in enumerate(X_LOADS):
                if n == 2:
                    sp.dma_start(w_raw[:, :, :], weights[0].rearrange("(k p) n -> p k n", p=P)).then_inc(w_in[0], 16)
                sp.dma_start(h_nat[:, first:end, :],
                             x[first * P:end * P, :].rearrange("(t p) d -> p t d", p=P)).then_inc(x_in[n], 16)

            def load_adj(i, par):
                sp.dma_start(adj_sb[:, par, :], adj[bass.ds(i * P, P), :]).then_inc(adj_in[par], 16)

            load_adj(0, 0)
            load_adj(1, 1)
            sp.wait_ge(w_lo, 1)
            sp.dma_start(w_raw[:, :, :], weights[1].rearrange("(k p) n -> p k n", p=P)).then_inc(w_in[1], 16)

            def next_adj(layer, i, par):
                sp.wait_ge(mask_done, CHUNKS * (layer * TILES + i - 1))
                load_adj(i, par)

            two(sp, 2, TILES - 1, lambda i, par: next_adj(0, i, par))

            def load_x(i, par):
                sp.dma_start(x_tile[:, par, :], x[bass.ds(i * P, P), :]).then_inc(xt_in[par], 16)

            def store(i, par):
                sp.wait_ge(h_ready, TILES + i + 1)
                sp.dma_start(out[bass.ds(i * P, P), :], h_new[:, par, :]).then_inc(stored[par], 16)

            load_x(0, 0)
            load_x(1, 1)
            next_adj(1, 0, 0)
            next_adj(1, 1, 1)
            next_adj(1, 2, 0)
            next_adj(1, 3, 1)
            store(0, 0)
            load_x(2, 0)

            def step(i, par):
                next_adj(1, i, par)
                store(i - 3, 1 - par)
                load_x(i - 1, 1 - par)

            two(sp, 4, TILES - 1, step)
            store(TILES - 3, 1)
            load_x(TILES - 1, 1)
            store(TILES - 2, 0)
            store(TILES - 1, 1)
            for b in range(2):
                sp.wait_ge(stored[b], 16 * (TILES // 2))

        @block.gpsimd
        def _(pool):
            nc.gpsimd.memset(ident[:, :], 0.0).then_inc(ident_done, 1)
            pool.wait_ge(ident_done, 1)
            nc.gpsimd.affine_select(out=ident[:, :], in_=ident[:, :], compare_op=ALU.not_equal, fill=1.0,
                                    base=0, pattern=[[-1, P]], channel_multiplier=1).then_inc(ident_done, 1)

            def save_h(i, par):
                pool.wait_ge(h_ready, i + 1)
                nc.gpsimd.tensor_copy(h_nat[:, bass.ds(i, 1), :].rearrange("p a d -> p (a d)"),
                                      h_new[:, par, :]).then_inc(saved, 1)

            def take_tile(layer, i, par):
                if not (layer == 0 and isinstance(i, int) and i < 2):
                    pool.wait_ge(scores_done, CHUNKS * (layer * TILES + i - 1))
                nc.gpsimd.tensor_copy(
                    wh_tile[:, par, :, :, :].rearrange("p h k n -> p (h k) n"),
                    hT[:, :, :, bass.ds(i * P, P)].rearrange("p h k n -> p (h k) n")).then_inc(tile_ready, 1)

            for layer in range(LAYERS):
                pool.wait_ge(proj_lo, 4 * CHUNKS * layer + 4)
                take_tile(layer, 0, 0)
                take_tile(layer, 1, 1)
                pool.wait_ge(proj_lo, 4 * CHUNKS * (layer + 1))
                if layer == 0:
                    def step(i, par):
                        take_tile(0, i, par)
                        save_h(i - 2, par)

                    two(pool, 2, TILES - 1, step)
                    save_h(TILES - 2, 0)
                    save_h(TILES - 1, 1)
                else:
                    two(pool, 2, TILES - 1, lambda i, par: take_tile(1, i, par))

        @block.tensor
        def _(pe):
            def transpose_pair(u):
                pe.wait_ge(ln_ready, 2 * u + 2)
                if u >= 2:
                    pe.wait_ge(pair_lo, u - 1)
                for t in range(2):
                    for k in range(KD):
                        last = nc.tensor.transpose(pair_bank(u)[:, k, t * P:(t + 1) * P],
                                                   h_nat[:, 2 * u + t, k * P:(k + 1) * P], ident[:, :])
                last.then_inc(pair_done, 1)

            def transpose_h(i, par):
                pe.wait_ge(h_ready, i + 1)
                for k in range(KD):
                    last = nc.tensor.transpose(hTbank(par)[:, k * P:(k + 1) * P],
                                               h_new[:, par, k * P:(k + 1) * P], ident[:, :])
                last.then_inc(hT_done, 1)

            def proj_bank(layer, c, b):
                if b == 0:
                    if layer:
                        pe.wait_ge(hT_lo, TPC * (c + 1))
                    else:
                        pe.wait_ge(pair_lo, TPC // 2 * (c + 1))
                    if c == 0:
                        pe.wait_ge(w_lo, layer + 1)
                if c == 0 and layer:
                    pe.wait_ge(exp_done, CHUNKS * (TILES * layer - 1) + b + 1)
                if c > 0:
                    pe.wait_ge(proj_lo, 4 * (CHUNKS * layer + c - 1) + b + 1)
                m = (b + KD) % (2 * KD)
                n = 0
                for k in range(KD):
                    for wh, mh in PASSES:
                        last = nc.tensor.matmul(ps[:, b, :], w_hl[:, wh, k, m * P:(m + 1) * P],
                                                hT[:, mh, k, c * BANK:(c + 1) * BANK],
                                                start=(n == 0), stop=(n == KD * len(PASSES) - 1))
                        n += 1
                last.then_inc(proj_done, 1)

            def nat(layer, i):
                pe.wait_ge(proj_lo, 4 * (CHUNKS * layer + i // TPC + 1))
                if i >= 2:
                    pe.wait_ge(nat_out, TILES * layer + i - 1)
                elif layer:
                    pe.wait_ge(pT_lo, 4 * TILES * layer)
                dst = tbank(i).bitcast(F32R)
                for n, (half, k) in enumerate(((HI, 0), (HI, 1), (LO, 0), (LO, 1))):
                    last = nc.tensor.transpose(dst[:, n * P:(n + 1) * P], hT[:, half, k, i * P:(i + 1) * P],
                                               ident_r[:, :])
                last.then_inc(nat_done, 1)

            def project(layer, c, between=lambda b: None):
                for b in range(4):
                    proj_bank(layer, c, b)
                    if c and b:
                        nat(layer, TPC * (c - 1) + b - 1)
                    between(b)
                if c:
                    nat(layer, TPC * c - 1)

            def score_chunk(layer, i, par, q):
                if q == 0:
                    pe.wait_ge(tile_ready, TILES * layer + i + 1)
                if score_bank(i, q) != q:
                    if layer:
                        pe.wait_ge(hT_lo, TILES)
                    else:
                        pe.wait_ge(pair_lo, TILES // 2)
                elif not (isinstance(i, int) and i == 0):
                    pe.wait_ge(exp_done, CHUNKS * (TILES * layer + i - 1) + q + 1)
                else:
                    pe.wait_ge(proj_lo, 4 * (CHUNKS * (layer + 1) - 1) + max(q + 1, 2 if q == CHUNKS - 1 else 0))
                n = 0
                for k in range(KD):
                    for sh, mh in PASSES:
                        last = nc.tensor.matmul(ps[:, score_bank(i, q), :], wh_tile[:, par, sh, k, :],
                                                wsT[:, mh, k, q * BANK:(q + 1) * BANK],
                                                start=(n == 0), stop=(n == KD * len(PASSES) - 1))
                        n += 1
                last.then_inc(scores_done, 1)

            def transpose_group(layer, i, par, q):
                g = TILES * layer + i
                pe.wait_ge(mask_done, CHUNKS * g + q + 1)
                if isinstance(i, int) and i == 0 and q < 2:
                    pe.wait_ge(nat_out, (layer + 1) * TILES)
                else:
                    pe.wait_ge(pT_lo, 4 * g + q - 1)
                for t in range(TPC):
                    j = q * TPC + t
                    last = nc.tensor.transpose(tbank(q)[:, t * P:(t + 1) * P],
                                               probs[:, par, j * P:(j + 1) * P], ident[:, :])
                last.then_inc(tr_done, 1)

            def product_quarter(layer, i, par, q):
                g = TILES * layer + i
                pe.wait_ge(pT_lo, 4 * g + q + 1)
                if q == 0:
                    if not (isinstance(i, int) and i < 2):
                        pe.wait_ge(h_ready, g - 1)
                        if layer == 0:
                            pe.wait_ge(hT_lo, i - 1)
                    elif layer:
                        pe.wait_ge(hT_lo, TILES)
                for t in range(TPC):
                    j = q * TPC + t
                    for n, (sh, mh) in enumerate(PASSES):
                        last = nc.tensor.matmul(prod(par), pT[:, sh, j, :], wh_nat[:, j, mh, :],
                                                start=(j == 0 and n == 0),
                                                stop=(j == TILES - 1 and n == len(PASSES) - 1))
                if q == CHUNKS - 1:
                    last.then_inc(prod_done, 1)

            def cycle(layer, i, par, head, with_hT=True):
                head(0)
                head(1)
                transpose_group(layer, i - 1, 1 - par, 0)
                head(2)
                if with_hT:
                    transpose_h(i - 2, par)
                transpose_group(layer, i - 1, 1 - par, 1)
                head(3)
                transpose_group(layer, i - 1, 1 - par, 2)
                product_quarter(layer, i - 1, 1 - par, 0)
                transpose_group(layer, i - 1, 1 - par, 3)
                for q in range(1, CHUNKS):
                    product_quarter(layer, i - 1, 1 - par, q)

            pe.wait_ge(ident_done, 2)
            pe.wait_ge(identr_done, 1)
            transpose_pair(0)
            transpose_pair(1)
            for c in range(CHUNKS):
                def next_pairs(b):
                    if c + 1 < CHUNKS and b in (1, 2):
                        transpose_pair(2 * (c + 1) + b - 1)

                project(0, c, next_pairs)
            for layer in range(LAYERS):
                score_chunk(layer, 0, 0, 0)
                score_chunk(layer, 0, 0, 1)
                nat(layer, TILES - 4)
                score_chunk(layer, 0, 0, 2)
                nat(layer, TILES - 3)
                score_chunk(layer, 0, 0, 3)
                nat(layer, TILES - 2)
                nat(layer, TILES - 1)
                cycle(layer, 1, 1, lambda q: score_chunk(layer, 1, 1, q), with_hT=False)
                two(pe, 2, TILES - 1,
                    lambda i, par: cycle(layer, i, par, lambda q: score_chunk(layer, i, par, q), with_hT=layer == 0))
                if layer + 1 < LAYERS:
                    cycle(layer, TILES, 0, lambda q: proj_bank(layer + 1, 0, q))
                    project(layer + 1, 1, lambda b: transpose_h(TILES - 1, 1) if b == 1 else None)
                    for c in range(2, CHUNKS):
                        project(layer + 1, c)
                else:
                    cycle(layer, TILES, 0, lambda q: None, with_hT=False)

        @block.scalar
        def _(act):
            def copy(dst, src):
                return nc.scalar.activation(dst, src, ACT.Copy)

            def split_w(layer):
                act.wait_ge(w_in[layer], 16)
                if layer:
                    act.wait_ge(proj_done, 4 * CHUNKS)
                copy(w_hl[:, HI, :, :], w_raw[:, :, :]).then_inc(w_hi, 1)

            def hi_pair(u):
                act.wait_ge(pair_done, u + 1)
                copy(hT[:, HI, :, 2 * u * P:2 * (u + 1) * P], pair_bank(u)).then_inc(pair_hi, 1)

            def hi_hT(i, par):
                act.wait_ge(hT_done, i + 1)
                copy(hT[:, HI, :, bass.ds(i * P, P)],
                     hTbank(par).rearrange("p (k n) -> p k n", k=KD)).then_inc(hT_hi, 1)

            def hi_proj(layer, c, b):
                act.wait_ge(proj_done, 4 * (CHUNKS * layer + c) + (b + 1 if b < 2 else 4))
                dst = wsT if b < KD else hT
                copy(dst[:, HI, b % KD, c * BANK:(c + 1) * BANK], ps[:, b, :]).then_inc(proj_hi, 1)

            def nat(layer, i):
                act.wait_ge(nat_done, TILES * layer + i + 1)
                copy(wh_nat[:, i, :, :].rearrange("p h d -> p (h d)"), tbank(i)).then_inc(nat_out, 1)

            def project(layer, c, between=lambda b: None):
                for b in range(4):
                    if b < KD:
                        hi_proj(layer, c, b)
                    if c and b:
                        nat(layer, TPC * (c - 1) + b - 1)
                    between(b)
                hi_proj(layer, c, 2)
                hi_proj(layer, c, 3)
                if c:
                    nat(layer, TPC * c - 1)

            def exps(layer, i, par, q):
                if q == 0:
                    act.wait_ge(max_done, TILES * layer + i + 1)
                nc.scalar.activation(probs[:, par, q * BANK:(q + 1) * BANK], ps[:, score_bank(i, q), :], ACT.Exp, bias=negmax[:, :],
                                     accum_out=chunksum[:, par, q:q + 1]).then_inc(exp_done, 1)

            def hi_pT(layer, i, q):
                g = TILES * layer + i
                act.wait_ge(tr_done, 4 * g + q + 1)
                if q == 0 and not (layer == 0 and isinstance(i, int) and i == 0):
                    act.wait_ge(prod_done, g)
                copy(pT[:, HI, q * TPC:(q + 1) * TPC, :].rearrange("p j n -> p (j n)"), tbank(q)).then_inc(pT_hi, 1)

            def cycle(layer, i, par, with_hT=True, with_scores=True):
                hi_pT(layer, i - 1, 0)
                if with_hT:
                    hi_hT(i - 2, par)
                hi_pT(layer, i - 1, 1)
                hi_pT(layer, i - 1, 2)
                if with_scores:
                    exps(layer, i, par, 0)
                    exps(layer, i, par, 1)
                hi_pT(layer, i - 1, 3)
                if with_scores:
                    exps(layer, i, par, 2)
                    exps(layer, i, par, 3)


            def root(c):
                act.wait_ge(vareps_done, c + 1)
                nc.scalar.activation(std0[:, c, :], var_eps[:, c, :], ACT.Sqrt).then_inc(sqrt_done, 1)

            def relu(c):
                act.wait_ge(shift_done, c + 1)
                for t in range(TPC):
                    i = TPC * c + t
                    nc.scalar.activation(h_nat[:, i, :], h_nat[:, i, :], ACT.Relu, bias=shift[:, c, t:t + 1],
                                         scale=rstd[:, c, t:t + 1]).then_inc(ln_ready, 1)

            root(0)
            split_w(0)
            relu(0)
            hi_pair(0)
            hi_pair(1)
            root(1)
            relu(1)
            for c in range(CHUNKS):
                def next_pairs(b):
                    if c + 2 < CHUNKS and b == 1:
                        root(c + 2)
                    if c + 1 < CHUNKS and b in (1, 2):
                        hi_pair(2 * (c + 1) + b - 1)
                    if c + 2 < CHUNKS and b == 3:
                        relu(c + 2)

                project(0, c, next_pairs)
            nc.scalar.activation(warm[:, :], rstd[:, 0, 0:1], ACT.Exp)
            for layer in range(LAYERS):
                nat(layer, TILES - 4)
                nat(layer, TILES - 3)
                nat(layer, TILES - 2)
                exps(layer, 0, 0, 0)
                nat(layer, TILES - 1)
                for q in range(1, CHUNKS):
                    exps(layer, 0, 0, q)
                cycle(layer, 1, 1, with_hT=False)
                if layer + 1 < LAYERS:
                    split_w(layer + 1)
                two(act, 2, TILES - 1, lambda i, par: cycle(layer, i, par, with_hT=layer == 0))
                if layer + 1 < LAYERS:
                    hi_proj(layer + 1, 0, 0)
                    hi_proj(layer + 1, 0, 1)
                    hi_pT(layer, TILES - 1, 0)
                    hi_hT(TILES - 2, 0)
                    hi_pT(layer, TILES - 1, 1)
                    hi_proj(layer + 1, 0, 2)
                    hi_proj(layer + 1, 0, 3)
                    hi_pT(layer, TILES - 1, 2)
                    hi_pT(layer, TILES - 1, 3)
                    project(layer + 1, 1, lambda b: hi_hT(TILES - 1, 1) if b == 1 else None)
                    for c in range(2, CHUNKS):
                        project(layer + 1, c)
                else:
                    cycle(layer, TILES, 0, with_hT=False, with_scores=False)

        @block.vector
        def _(dve):
            def rest(dst, src, hi):
                return nc.vector.tensor_tensor(dst, src, bits(hi), ALU.subtract)

            def split_w(layer):
                dve.wait_ge(w_hi, layer + 1)
                rest(w_hl[:, LO, :, :].rearrange("p k n -> p (k n)"), w_raw[:, :, :].rearrange("p k n -> p (k n)"),
                     w_hl[:, HI, :, :].rearrange("p k n -> p (k n)")).then_inc(w_lo, 1)

            def lo_pair(u):
                dve.wait_ge(pair_hi, u + 1)
                cols = slice(2 * u * P, 2 * (u + 1) * P)
                rest(hT[:, LO, :, cols], pair_bank(u), hT[:, HI, :, cols]).then_inc(pair_lo, 1)

            def lo_hT(i, par):
                dve.wait_ge(hT_hi, i + 1)
                rest(hT[:, LO, :, bass.ds(i * P, P)], hTbank(par).rearrange("p (k n) -> p k n", k=KD),
                     hT[:, HI, :, bass.ds(i * P, P)]).then_inc(hT_lo, 1)

            def lo_proj(layer, c, b):
                dve.wait_ge(proj_hi, 4 * (CHUNKS * layer + c) + b + 1)
                dst = wsT if b < KD else hT
                cols = slice(c * BANK, (c + 1) * BANK)
                rest(dst[:, LO, b % KD, cols], ps[:, b, :], dst[:, HI, b % KD, cols]).then_inc(proj_lo, 1)

            def project(layer, c, between=lambda b: None):
                for b in range(4):
                    if b < KD:
                        lo_proj(layer, c, b)
                    between(b)
                lo_proj(layer, c, 2)
                lo_proj(layer, c, 3)

            def maxima(layer, i, q):
                n = CHUNKS * (TILES * layer + i) + q + 1
                dve.wait_ge(scores_done, n)
                nc.vector.tensor_reduce(chunkmax[:, q:q + 1], ps[:, score_bank(i, q), :], AX.X, ALU.max).then_inc(chunkmax_done, 1)
                if q == CHUNKS - 1:
                    dve.wait_ge(chunkmax_done, n)
                    nc.vector.tensor_reduce(negmax[:, :], chunkmax[:, :], AX.X, ALU.max,
                                            negate=True).then_inc(max_done, 1)

            def mask(layer, i, par, q):
                g = TILES * layer + i
                dve.wait_ge(exp_done, CHUNKS * g + q + 1)
                if q == 0:
                    dve.wait_ge(adj_in[par], 8 * (g - par) + 16)
                cols = slice(q * BANK, (q + 1) * BANK)
                nc.vector.tensor_tensor(probs[:, par, cols], probs[:, par, cols], adj_sb[:, par, cols],
                                        ALU.mult).then_inc(mask_done, 1)

            def norms(layer, i, par):
                g = TILES * layer + i
                nc.vector.tensor_reduce(rowsum[:, :], chunksum[:, par, :], AX.X, ALU.add).then_inc(rowsum_done, 1)
                dve.wait_ge(rowsum_done, g + 1)
                nc.vector.reciprocal(rinv[:, par, :], rowsum[:, :]).then_inc(rinv_done, 1)

            def lo_pT(layer, i, q):
                dve.wait_ge(pT_hi, 4 * (TILES * layer + i) + q + 1)
                js = slice(q * TPC, (q + 1) * TPC)
                rest(pT[:, LO, js, :].rearrange("p j n -> p (j n)"), tbank(q),
                     pT[:, HI, js, :].rearrange("p j n -> p (j n)")).then_inc(pT_lo, 1)

            def tail(layer, i, par):
                g = TILES * layer + i
                dve.wait_ge(rinv_done, g + 1)
                dve.wait_ge(prod_done, g + 1)
                nc.vector.scalar_tensor_tensor(
                    out=z[:, :], in0=prod(par), scalar=rinv[:, par, :],
                    in1=h_nat[:, bass.ds(i, 1), :].rearrange("p a d -> p (a d)"),
                    op0=ALU.mult, op1=ALU.add).then_inc(z_done, 1)
                dve.wait_ge(z_done, g + 1)
                early = isinstance(i, int) and i < 2
                if layer == 0:
                    if not early:
                        dve.wait_ge(hT_done, i - 1)
                        dve.wait_ge(saved, i - 1)
                elif early:
                    dve.wait_ge(hT_done, TILES)
                    dve.wait_ge(saved, TILES)
                else:
                    dve.wait_ge(stored[par], 8 * (i - par))
                ins = nc.vector.scalar_tensor_tensor(out=h_new[:, par, :], in0=z[:, :], scalar=SLOPE, in1=z[:, :],
                                                     op0=ALU.mult, op1=ALU.max)
                if layer + 1 < LAYERS:
                    ins.then_inc(h_ready, 1)
                else:
                    ins.then_inc(leaky_done, 1)
                    dve.wait_ge(leaky_done, i + 1)
                    dve.wait_ge(xt_in[par], 8 * (i - par) + 16)
                    nc.vector.tensor_tensor(h_new[:, par, :], h_new[:, par, :], x_tile[:, par, :],
                                            ALU.add).then_inc(h_ready, 1)

            def cycle(layer, i, par, with_tail=True):
                if with_tail:
                    tail(layer, i - 2, par)
                maxima(layer, i, 0)
                maxima(layer, i, 1)
                lo_pT(layer, i - 1, 0)
                maxima(layer, i, 2)
                if with_tail and layer == 0:
                    lo_hT(i - 2, par)
                lo_pT(layer, i - 1, 1)
                maxima(layer, i, 3)
                lo_pT(layer, i - 1, 2)
                mask(layer, i, par, 0)
                mask(layer, i, par, 1)
                lo_pT(layer, i - 1, 3)
                mask(layer, i, par, 2)
                mask(layer, i, par, 3)
                norms(layer, i, par)

            dve.wait_ge(ident_done, 2)
            nc.vector.tensor_copy(ident_r[:, :], ident[:, :]).then_inc(identr_done, 1)

            def norm(c):
                for t in range(TPC):
                    for n, (first, end) in enumerate(X_LOADS):
                        if first == TPC * c + t:
                            dve.wait_ge(x_in[n], 16)
                    nc.vector.bn_stats(stats[:, c, t, :], h_nat[:, TPC * c + t, :]).then_inc(stats_done, 1)
                for t in range(TPC):
                    dve.wait_ge(stats_done, TPC * c + t + 1)
                    nc.vector.bn_aggr(meanvar[:, c, t, :], stats[:, c, t, :]).then_inc(aggr_done, 1)
                dve.wait_ge(aggr_done, TPC * (c + 1))
                nc.vector.tensor_scalar_add(var_eps[:, c, :], meanvar[:, c, :, 1], EPS).then_inc(vareps_done, 1)

            def affine(c):
                dve.wait_ge(sqrt_done, c + 1)
                nc.vector.reciprocal(std_inv0[:, c, :], std0[:, c, :]).then_inc(newton_done, 1)
                dve.wait_ge(newton_done, 4 * c + 1)
                nc.vector.scalar_tensor_tensor(out=quot[:, c, :], in0=var_eps[:, c, :], scalar=0.5,
                                               in1=std_inv0[:, c, :], op0=ALU.mult, op1=ALU.mult).then_inc(newton_done, 1)
                dve.wait_ge(newton_done, 4 * c + 2)
                nc.vector.scalar_tensor_tensor(out=std[:, c, :], in0=std0[:, c, :], scalar=0.5,
                                               in1=quot[:, c, :], op0=ALU.mult, op1=ALU.add).then_inc(newton_done, 1)
                dve.wait_ge(newton_done, 4 * c + 3)
                nc.vector.reciprocal(rstd[:, c, :], std[:, c, :]).then_inc(newton_done, 1)
                dve.wait_ge(newton_done, 4 * c + 4)
                nc.vector.scalar_tensor_tensor(out=shift[:, c, :], in0=meanvar[:, c, :, 0], scalar=-1.0,
                                               in1=rstd[:, c, :], op0=ALU.mult, op1=ALU.mult).then_inc(shift_done, 1)

            norm(0)
            affine(0)
            split_w(0)
            norm(1)
            lo_pair(0)
            lo_pair(1)
            affine(1)
            for c in range(CHUNKS):
                def next_pairs(b):
                    if c + 2 < CHUNKS and b == 0:
                        norm(c + 2)
                    if c + 2 < CHUNKS and b == 1:
                        affine(c + 2)
                    if c + 1 < CHUNKS and b in (1, 2):
                        lo_pair(2 * (c + 1) + b - 1)

                project(0, c, next_pairs)
            for layer in range(LAYERS):
                for q in range(CHUNKS):
                    maxima(layer, 0, q)
                for q in range(CHUNKS):
                    mask(layer, 0, 0, q)
                norms(layer, 0, 0)
                cycle(layer, 1, 1, with_tail=False)
                if layer + 1 < LAYERS:
                    split_w(layer + 1)
                cycle(layer, 2, 0)
                cycle(layer, 3, 1)
                two(dve, 4, TILES - 1, lambda i, par: cycle(layer, i, par))
                if layer + 1 < LAYERS:
                    tail(layer, TILES - 2, 0)
                    lo_proj(layer + 1, 0, 0)
                    lo_proj(layer + 1, 0, 1)
                    lo_pT(layer, TILES - 1, 0)
                    lo_hT(TILES - 2, 0)
                    lo_pT(layer, TILES - 1, 1)
                    lo_proj(layer + 1, 0, 2)
                    lo_proj(layer + 1, 0, 3)
                    lo_pT(layer, TILES - 1, 2)
                    lo_pT(layer, TILES - 1, 3)
                    tail(layer, TILES - 1, 1)
                    project(layer + 1, 1, lambda b: lo_hT(TILES - 1, 1) if b == 1 else None)
                    for c in range(2, CHUNKS):
                        project(layer + 1, c)
                else:
                    lo_pT(layer, TILES - 1, 0)
                    lo_pT(layer, TILES - 1, 1)
                    tail(layer, TILES - 2, 0)
                    lo_pT(layer, TILES - 1, 2)
                    lo_pT(layer, TILES - 1, 3)
                    tail(layer, TILES - 1, 1)


def kernel(x, adj, L0_gnn_W_stack):
    import numpy as np
    import concourse.bacc as bacc
    from concourse.bass_utils import run_bass_kernel_spmd

    nc = bacc.Bacc("TRN2", target_bir_lowering=False, num_devices=1)
    arrays = {"x": np.ascontiguousarray(x), "adj": np.ascontiguousarray(adj),
              "weights": np.ascontiguousarray(L0_gnn_W_stack)}
    aps = [nc.dram_tensor(n, a.shape, mybir.dt.from_np(a.dtype), kind="ExternalInput").ap()
           for n, a in arrays.items()]
    out = nc.dram_tensor("out", (N, D), F32, kind="ExternalOutput").ap()
    gat_kernel(nc, *aps, out)
    result = run_bass_kernel_spmd(nc, [arrays], core_ids=[0])
    return result.results[0]["out"]
```
